# Optimizing a Trainium2 kernel written in Bass

```python
import numpy as np
import jax
import jax.numpy as jnp

def _softmax(x, axis=-1):
    return jax.nn.softmax(x, axis=axis)

def _gelu(x):
    return jax.nn.gelu(x, approximate=True)

def _silu(x):
    return jax.nn.silu(x)

def _sigmoid(x):
    return jax.nn.sigmoid(x)

def _layernorm(x, axis=-1, eps=1e-05):
    m = jnp.mean(x, axis=axis, keepdims=True)
    v = jnp.var(x, axis=axis, keepdims=True)
    return (x - m) / jnp.sqrt(v + eps)

def _scatter_add(tgt, idx, src, axis=0):
    return tgt.at[idx].add(src)

def _segment_sum(src, seg, n):
    return jax.ops.segment_sum(src, seg, n)
kernel_name = 'mk_rec_standalone_d1_rec_r8_619559'

def setup_inputs(seed: int=0):
    np.random.seed(seed)
    _w = jnp.asarray

    def _rec_inputs():
        import jax
        import jax.numpy as jnp
        _rk = jax.random.key(seed)
        r_x = -0.00154741 + 1.00114 * jax.random.normal(jax.random.fold_in(_rk, 1), (512, 64), jnp.float32)
        return r_x
    r_x = _rec_inputs()

    def _L0_rec_setup():
        import jax, jax.numpy as jnp
        import numpy as np
        import itertools
        LN_EPS = 1e-05

        def _combo_idx(d):
            pairs = np.array(list(itertools.combinations(range(d), 2)), dtype=np.int32)
            trips = np.array(list(itertools.combinations(range(d), 3)), dtype=np.int32)
            return (pairs, trips)
        key = jax.random.key(seed)
        k1, k2 = jax.random.split(key)
        d, batch, out_dim = (64, 512, 512)
        total = d + d * (d - 1) // 2 + d * (d - 1) * (d - 2) // 6
        x = jax.random.normal(k1, (batch, d), dtype=jnp.float32)
        W = jax.random.normal(k2, (total, out_dim), dtype=jnp.float32) * (1.0 / np.sqrt(total))
        b = jnp.zeros((out_dim,), dtype=jnp.float32)
        gamma = jnp.ones((out_dim,), dtype=jnp.float32)
        beta = jnp.zeros((out_dim,), dtype=jnp.float32)
        return {'x': x, 'W': W, 'b': b, 'gamma': gamma, 'beta': beta}
    _L0_rec_all = _L0_rec_setup()
    _L0_rec_in = {k: v for k, v in _L0_rec_all.items() if k in ('W', 'b', 'gamma', 'beta')}
    del _L0_rec_all
    return {'r_x': r_x, 'L0_rec_W': _L0_rec_in['W'], 'L0_rec_b': _L0_rec_in['b'], 'L0_rec_gamma': _L0_rec_in['gamma'], 'L0_rec_beta': _L0_rec_in['beta']}

def reference(r_x, L0_rec_W, L0_rec_b, L0_rec_gamma, L0_rec_beta):
    import jax
    import jax.numpy as jnp

    def _L0_rec_ref(x, W, b, gamma, beta):
        import jax, jax.numpy as jnp
        import numpy as np
        import itertools
        LN_EPS = 1e-05

        def _combo_idx(d):
            pairs = np.array(list(itertools.combinations(range(d), 2)), dtype=np.int32)
            trips = np.array(list(itertools.combinations(range(d), 3)), dtype=np.int32)
            return (pairs, trips)
        d = x.shape[1]
        pairs, trips = _combo_idx(d)
        pw = x[:, pairs[:, 0]] * x[:, pairs[:, 1]]
        tp = x[:, trips[:, 0]] * x[:, trips[:, 1]] * x[:, trips[:, 2]]
        feats = jnp.concatenate([x, pw, tp], axis=1)
        h = feats @ W + b
        mu = jnp.mean(h, axis=-1, keepdims=True)
        var = jnp.var(h, axis=-1, keepdims=True)
        hn = (h - mu) * jax.lax.rsqrt(var + LN_EPS) * gamma + beta
        return jax.nn.relu(hn)
    y = _L0_rec_ref(r_x, L0_rec_W, L0_rec_b, L0_rec_gamma, L0_rec_beta)
    return y

_drawn_inputs = setup_inputs


def setup_inputs(seed=0):
    import zlib

    import numpy as np

    out = dict(_drawn_inputs(seed))
    spreads = {'L0_rec_b': (0.0, 0.1), 'L0_rec_gamma': (1.0, 0.2), 'L0_rec_beta': (0.0, 0.1)}
    factors = {}
    for name, (base, spread) in spreads.items():
        noise = np.random.default_rng([zlib.crc32(name.encode()), seed]).standard_normal(out[name].shape)
        drawn = base * np.exp(spread * noise) if base else spread * noise
        out[name] = jnp.asarray(drawn.astype(out[name].dtype))
    for name, factor in factors.items():
        out[name] = (out[name] * factor).astype(out[name].dtype)
    return out
```

```python
from contextlib import ExitStack

import concourse.bass as bass
from concourse import mybir

F32 = mybir.dt.float32
F32R = mybir.dt.float32r
ALU = mybir.AluOpType
ACT = mybir.ActivationFunctionType
EPS = 1e-5

D, BATCH, OUT = 64, 512, 512
P = 128
BT = BATCH // P
PAIRS = D * (D - 1) // 2
TRIPLES = D * (D - 1) * (D - 2) // 6
TOTAL = D + PAIRS + TRIPLES
PT = -(-PAIRS // P)
LEAD = PT * P - PAIRS


def n_pairs(i):
    return (D - 1 - i) * (D - 2 - i) // 2


def first_pair(i):
    return PAIRS - (D - i) * (D - 1 - i) // 2


def first_triple(i):
    return TOTAL - (D - i) * (D - 1 - i) * (D - 2 - i) // 6


GROUPS = sum(n_pairs(i) >= P for i in range(D))
SEGMENTS = []
_tiles = 0
for _n in range(1, PT):
    _gs = [g for g in range(GROUPS) if n_pairs(GROUPS - 1 - g) // P == _n]
    SEGMENTS.append((_n, _gs[0], len(_gs), _tiles))
    _tiles += _n * len(_gs)
PAIR_TILE0 = _tiles
PACK_TILE0 = PAIR_TILE0 + PT

RUNS = [(0, D - LEAD, 0, None, None)]
_row = D - LEAD
for _i in range(D - 2):
    _rows = n_pairs(_i) % P
    if _rows:
        RUNS.append((_row, _rows, first_triple(_i), _i, LEAD + first_pair(_i + 1)))
        _row += _rows
PACKED = _row
PACKS = -(-PACKED // P)
LAST_ROWS = PACKED - (PACKS - 1) * P


def pieces(tile):
    out = []
    for at, rows, w, x, p in RUNS:
        lo, hi = max(at, tile * P), min(at + rows, (tile + 1) * P)
        if lo < hi:
            out.append((lo - tile * P, hi - lo, w + lo - at, x, None if p is None else p + lo - at))
    return out


def pair_runs(tile):
    out = []
    for j in range(D - 1):
        at = LEAD + first_pair(j)
        lo, hi = max(at, tile * P), min(at + D - 1 - j, (tile + 1) * P)
        if lo < hi:
            out.append((lo - tile * P, hi - lo, j, j + 1 + lo - at))
    return out


RING = 8
GATHER = 3
FSLOTS = 2
PACK_BATCH = PT
BATCHES = -(-PACKS // PACK_BATCH)


def build(nc, x, x_t, w, b, gamma, beta, out):
    ctx = ExitStack()
    with ctx:
        def sb(name, shape, dt=F32):
            return ctx.enter_context(nc.sbuf_tensor(name, shape, dt))

        def sem(name):
            return ctx.enter_context(nc.semaphore(name))

        p_hi = sb("p_hi", [P, PT, BATCH], F32R)
        p_lo = sb("p_lo", [P, PT, BATCH], F32R)
        w_raw = sb("w_raw", [P, 2, PT, OUT])
        w_hi = sb("w_hi", [P, RING, OUT], F32R)
        w_lo = sb("w_lo", [P, RING, OUT], F32R)
        left = sb("left", [P, GATHER, BATCH])
        right = sb("right", [P, GATHER, BATCH])
        prod = sb("prod", [P, GATHER, BATCH])
        f_hi = sb("f_hi", [P, FSLOTS, BATCH], F32R)
        f_lo = sb("f_lo", [P, FSLOTS, BATCH], F32R)
        acc = sb("acc", [P, BT, OUT])
        x_col = sb("x_col", [P, BT, D])
        b_all = sb("b_all", [P, OUT])
        gamma_all = sb("gamma_all", [P, OUT])
        beta_all = sb("beta_all", [P, OUT])
        stats = sb("stats", [P, BT, 6])
        mean_var = sb("mean_var", [P, BT, 2])
        small = sb("small", [P, BT, 6])
        psum = ctx.enter_context(nc.psum_tensor("psum", [P, 2 * BT, OUT], F32))
        p_list = nc.dram_tensor("p_list", (PT * P, BATCH), F32, kind="Internal").ap()

        consts_in = sem("consts_in")
        gathered = [sem(f"gathered{s}") for s in range(GATHER)]
        ones_set = sem("ones_set")
        prod_ready = sem("prod_ready")
        p_stored = sem("p_stored")
        feat_hi = sem("feat_hi")
        p_ready = sem("p_ready")
        f_ready = sem("f_ready")
        w_landed = sem("w_landed")
        pack_landed = [sem(f"pack_landed{s}") for s in range(BATCHES)]
        hi_ready = sem("hi_ready")
        lo_ready = sem("lo_ready")
        w_used = sem("w_used")
        drained = sem("drained")
        all_summed = [sem(f"all_summed{m}") for m in range(BT)]
        ln_step = sem("ln_step")
        veps_ready = sem("veps_ready")
        root_ready = sem("root_ready")
        normed = sem("normed")
        relu_done = sem("relu_done")
        stored = sem("stored")
        block = ctx.enter_context(nc.Block())

        gather_count = [0] * GATHER

        def gather_dmas(f):
            s = f % GATHER
            if f < PT:
                tile = PT - 1 - f
                dmas = []
                if tile == 0:
                    dmas.append((left[0:LEAD, s, :], x_t[D - LEAD:D, :]))
                for p0, rows, j, k in pair_runs(tile):
                    dmas.append((left[p0:p0 + rows, s, :], x_t[j:j + 1, :].to_broadcast([rows, BATCH])))
                    dmas.append((right[p0:p0 + rows, s, :], x_t[k:k + rows, :]))
                return dmas
            dmas = []
            for p0, rows, _, i, q in pieces(f - PT):
                if i is None:
                    dmas.append((left[p0:p0 + rows, s, :], x_t[0:rows, :]))
                else:
                    dmas.append((left[p0:p0 + rows, s, :], x_t[i:i + 1, :].to_broadcast([rows, BATCH])))
                    dmas.append((right[p0:p0 + rows, s, :], p_list[q:q + rows, :]))
            return dmas

        GATHER_DONE = []
        for f in range(PT + PACKS):
            gather_count[f % GATHER] += 16 * len(gather_dmas(f))
            GATHER_DONE.append(gather_count[f % GATHER])
        ONES = {PT - 1: 1, PT: 2}

        def row_of_full(g, n):
            a = g + (D - GROUPS)
            return TOTAL - a * (a - 1) * (a - 2) // 6 - n * P

        @block.sync
        def _(sp):
            def load(row, n, buf):
                src = w[bass.ds(row, n * P), :].rearrange("(t p) o -> p t o", p=P)
                sp.dma_start(w_raw[:, buf, 0:n, :], src).then_inc(w_landed, 16)

            before = []
            for n, g0, count, k0 in SEGMENTS:
                before += [k0 + n * c for c in range(count)]
            for n, g0, count, k0 in SEGMENTS:
                peel = count if g0 == 0 else 1
                for g in range(g0, g0 + peel):
                    if g >= 1:
                        sp.wait_ge(w_landed, 16 * g)
                    if g >= 2:
                        sp.wait_ge(lo_ready, before[g - 1])
                    load(row_of_full(g, n), n, g % 2)
                if count > peel:
                    with sp.Fori(g0 + peel, g0 + count) as g:
                        sp.wait_ge(w_landed, g * 16)
                        sp.wait_ge(lo_ready, (g - (g0 + 1)) * n + k0)
                        load(row_of_full(g, n), n, g % 2)
            sp.wait_ge(w_landed, 16 * GROUPS)
            sp.wait_ge(lo_ready, before[GROUPS - 1])
            sp.dma_start(w_raw[:, GROUPS % 2, :, :], w[D - LEAD:D - LEAD + PT * P, :].rearrange("(t p) o -> p t o", p=P)).then_inc(w_landed, 16)
            for batch in range(BATCHES):
                sp.wait_ge(lo_ready, PAIR_TILE0 + PT * batch)
                for tile in range(PACK_BATCH * batch, min(PACKS, PACK_BATCH * (batch + 1))):
                    for p0, rows, row, _, _ in pieces(tile):
                        sp.dma_start(w_raw[p0:p0 + rows, (GROUPS + 1 + batch) % 2, tile % PACK_BATCH, :],
                                     w[row:row + rows, :]).then_inc(pack_landed[batch], 16)
            for m in range(BT):
                sp.wait_ge(relu_done, m + 1)
                sp.dma_start(out[m * P:(m + 1) * P, :], right[:, m % 2, :] if m < 2 else prod[:, m % 2, :]).then_inc(stored, 16)
            sp.wait_ge(stored, 16 * BT)

        @block.gpsimd
        def _(pool):
            def ones(f, value):
                nc.gpsimd.memset(right[0:(LEAD if f < PT else D - LEAD), f % GATHER, :], 1.0).then_inc(ones_set, 1)

            def gather(f):
                if f >= GATHER:
                    pool.wait_ge(prod_ready, f - GATHER + 1)
                if f in ONES:
                    ones(f, 1.0)
                for dst, src in gather_dmas(f):
                    pool.dma_start(dst, src).then_inc(gathered[f % GATHER], 16)

            def store(f):
                tile = PT - 1 - f
                pool.wait_ge(prod_ready, f + 1)
                if f:
                    pool.wait_ge(p_stored, 16 * f)
                pool.dma_start(p_list[tile * P:(tile + 1) * P, :], prod[:, f % GATHER, :]).then_inc(p_stored, 16)

            gather(0)
            pool.dma_start(x_col[:], x.rearrange("(m p) d -> p m d", p=P)).then_inc(consts_in, 16)
            pool.dma_start(b_all[:], b.to_broadcast([P, OUT])).then_inc(consts_in, 16)
            gather(1)
            for f in range(2, PT):
                gather(f)
                store(f - 2)
            pool.dma_start(gamma_all[:], gamma.to_broadcast([P, OUT])).then_inc(consts_in, 16)
            pool.dma_start(beta_all[:], beta.to_broadcast([P, OUT])).then_inc(consts_in, 16)
            for f in range(PT - 2, PT):
                store(f)
            pool.wait_ge(p_stored, 16 * PT)
            for f in range(PT, PT + PACKS):
                gather(f)

        @block.scalar
        def _(act):
            def split_hi(raw, k, rows=P):
                act.wait_ge(w_used, k + 1)
                nc.scalar.copy(w_hi[0:rows, k % RING, :], raw).then_inc(hi_ready, 1)

            for n, g0, count, k0 in SEGMENTS:
                with act.Fori(g0, g0 + count) as g:
                    act.wait_ge(w_landed, g * 16 + 16)
                    for t in range(n):
                        split_hi(w_raw[:, g % 2, t, :], (g - g0) * n + (k0 + t))
            act.wait_ge(w_landed, 16 * (GROUPS + 1))
            for t in range(PT):
                split_hi(w_raw[:, GROUPS % 2, t, :], PAIR_TILE0 + t)
            for batch in range(BATCHES):
                tiles = range(PACK_BATCH * batch, min(PACKS, PACK_BATCH * (batch + 1)))
                act.wait_ge(pack_landed[batch], 16 * sum(len(pieces(t)) for t in tiles))
                for tile in tiles:
                    rows = P if tile < PACKS - 1 else LAST_ROWS
                    split_hi(w_raw[0:rows, (GROUPS + 1 + batch) % 2, tile % PACK_BATCH, :], PACK_TILE0 + tile, rows)
            for m in range(BT):
                act.wait_ge(veps_ready, m + 1)
                nc.scalar.activation(small[:, m, 1:2], small[:, m, 0:1], ACT.Sqrt).then_inc(root_ready, 1)

        @block.vector
        def _(dve):
            dve.sem_inc(drained, 2 * BT)

            steps = [0]

            def after(ins):
                steps[0] += 1
                ins.then_inc(ln_step, 1)
                dve.wait_ge(ln_step, steps[0])

            def split_lo(raw, k, rows=P):
                dve.wait_ge(hi_ready, k + 1)
                nc.vector.tensor_tensor(w_lo[0:rows, k % RING, :], raw, w_hi[0:rows, k % RING, :].bitcast(F32),
                                        ALU.subtract).then_inc(lo_ready, 1)

            def multiply(f, rows=P):
                s = f % GATHER
                dve.wait_ge(gathered[s], GATHER_DONE[f])
                if f in ONES:
                    dve.wait_ge(ones_set, ONES[f])
                if GATHER <= f < PT + GATHER:
                    dve.wait_ge(p_stored, 16 * (f - GATHER + 1))
                if f >= GATHER:
                    dve.wait_ge(prod_ready, f - GATHER + 1)
                nc.vector.tensor_tensor(prod[0:rows, s, :], left[0:rows, s, :], right[0:rows, s, :], ALU.mult).then_inc(prod_ready, 1)
                dve.wait_ge(prod_ready, f + 1)

            def split(f, hi, lo, ready, rows=P):
                s = f % GATHER
                nc.vector.tensor_copy(hi, prod[0:rows, s, :]).then_inc(feat_hi, 1)
                dve.wait_ge(feat_hi, f + 1)
                nc.vector.tensor_tensor(lo, prod[0:rows, s, :], hi.bitcast(F32), ALU.subtract).then_inc(ready, 1)

            def build_p(f):
                tile = PT - 1 - f
                multiply(f)
                split(f, p_hi[:, tile, :], p_lo[:, tile, :], p_ready)

            def drain(g, tiles, first=False):
                dve.wait_ge(w_used, tiles + RING)
                for m in range(BT):
                    if not first:
                        dve.wait_ge(drained, g * BT + (BT + m + 1))
                    nc.vector.scalar_tensor_tensor(
                        out=acc[:, m, :], in0=psum[:, (g % 2) * BT + m, :], scalar=x_col[:, m, bass.ds((GROUPS - 1) - g, 1)],
                        in1=b_all[:] if first else acc[:, m, :], op0=ALU.mult, op1=ALU.add).then_inc(drained, 1)

            def lo_of_group(g, n, g0, k0):
                for t in range(n):
                    split_lo(w_raw[:, g % 2, t, :], (g - g0) * n + (k0 + t))

            build_p(0)
            for n, g0, count, k0 in SEGMENTS:
                peel = 2 if g0 == 0 else 0
                if peel:
                    lo_of_group(0, n, g0, k0)
                    lo_of_group(1, n, g0, k0)
                    dve.wait_ge(consts_in, 32)
                    drain(0, 1, first=True)
                with dve.Fori(g0 + peel, g0 + count) as g:
                    lo_of_group(g, n, g0, k0)
                    drain(g - 1, (g - g0) * n + k0)
                build_p(n)
            for t in range(PT):
                split_lo(w_raw[:, GROUPS % 2, t, :], PAIR_TILE0 + t)
                if t == 0:
                    drain(GROUPS - 1, PAIR_TILE0)
            for tile in range(PACKS):
                rows = P if tile < PACKS - 1 else LAST_ROWS
                f, s = PT + tile, tile % FSLOTS
                multiply(f, rows)
                if tile >= FSLOTS:
                    dve.wait_ge(w_used, RING + PACK_TILE0 + tile - FSLOTS + 1)
                split(f, f_hi[0:rows, s, :], f_lo[0:rows, s, :], f_ready, rows)
                split_lo(w_raw[0:rows, (GROUPS + 1 + tile // PACK_BATCH) % 2, tile % PACK_BATCH, :], PACK_TILE0 + tile, rows)

            dve.wait_ge(consts_in, 64)
            dve.wait_ge(prod_ready, PT + PACKS)
            for m in range(BT):
                dve.wait_ge(all_summed[m], 1)
                h = acc[:, m, :]
                o = right[:, m % 2, :] if m < 2 else prod[:, m % 2, :]
                veps, root, y, yy, c, rstd = (small[:, m, c:c + 1] for c in range(6))
                dve.wait_ge(drained, (GROUPS + 1) * BT + m + 1)
                after(nc.vector.tensor_tensor(h, psum[:, (GROUPS % 2) * BT + m, :], h, ALU.add))
                after(nc.vector.bn_stats(stats[:, m, :], h))
                after(nc.vector.bn_aggr(mean_var[:, m, :], stats[:, m, :]))
                nc.vector.tensor_scalar(veps, mean_var[:, m, 1:2], EPS, None, ALU.add).then_inc(veps_ready, 1)
                after(nc.vector.scalar_tensor_tensor(out=o, in0=h, scalar=mean_var[:, m, 0:1], in1=gamma_all[:], op0=ALU.subtract, op1=ALU.mult))
                dve.wait_ge(root_ready, m + 1)
                after(nc.vector.reciprocal(y, root))
                after(nc.vector.scalar_tensor_tensor(out=yy, in0=y, scalar=veps, in1=y, op0=ALU.mult, op1=ALU.mult))
                after(nc.vector.tensor_scalar(c, yy, -0.5, 1.5, ALU.mult, ALU.add))
                after(nc.vector.tensor_tensor(rstd, y, c, ALU.mult))
                after(nc.vector.scalar_tensor_tensor(out=o, in0=o, scalar=rstd, in1=beta_all[:], op0=ALU.mult, op1=ALU.add))
                nc.vector.tensor_scalar(o, o, 0.0, None, ALU.max).then_inc(relu_done, 1)

        @block.tensor
        def _(pe):
            pe.sem_inc(w_used, RING)

            def k_tile(hi, lo, k, bank, start, stop, rows=P):
                wh = w_hi[0:rows, k % RING, :]
                wl = w_lo[0:rows, k % RING, :]
                for m in range(BT):
                    cols = slice(m * P, (m + 1) * P)
                    nc.tensor.matmul(psum[:, bank + m, :], hi[:, cols], wh, start=start, stop=False)
                    nc.tensor.matmul(psum[:, bank + m, :], hi[:, cols], wl, start=False, stop=False)
                    last = nc.tensor.matmul(psum[:, bank + m, :], lo[:, cols], wh, start=False, stop=stop)
                    if stop and m < BT - 1 and final:
                        last.then_inc(all_summed[m], 1)
                return last

            final = False
            for n, g0, count, k0 in SEGMENTS:
                pe.wait_ge(p_ready, n)
                with pe.Fori(g0, g0 + count) as g:
                    pe.wait_ge(drained, g * BT + BT)
                    for t in range(n):
                        k = (g - g0) * n + (k0 + t)
                        pe.wait_ge(lo_ready, k + 1)
                        last = k_tile(p_hi[:, PT - n + t, :], p_lo[:, PT - n + t, :], k, (g % 2) * BT, t == 0, t == n - 1)
                        last.then_inc(w_used, 1)
            bank = (GROUPS % 2) * BT
            pe.wait_ge(p_ready, PT)
            pe.wait_ge(drained, (GROUPS + 1) * BT)
            for t in range(PT):
                pe.wait_ge(lo_ready, PAIR_TILE0 + t + 1)
                k_tile(p_hi[:, t, :], p_lo[:, t, :], PAIR_TILE0 + t, bank, t == 0, False).then_inc(w_used, 1)
            for tile in range(PACKS):
                final = tile == PACKS - 1
                rows = LAST_ROWS if final else P
                pe.wait_ge(f_ready, tile + 1)
                pe.wait_ge(lo_ready, PACK_TILE0 + tile + 1)
                last = k_tile(f_hi[0:rows, tile % FSLOTS, :], f_lo[0:rows, tile % FSLOTS, :], PACK_TILE0 + tile, bank, False, final, rows)
                last.then_inc(all_summed[BT - 1] if final else w_used, 1)


def kernel(r_x, L0_rec_W, L0_rec_b, L0_rec_gamma, L0_rec_beta):
    import concourse.bacc as bacc
    import numpy as np
    from concourse.bass_utils import run_bass_kernel_spmd

    nc = bacc.Bacc("TRN2", target_bir_lowering=False, num_devices=1)
    r_x = np.asarray(r_x)
    arrays = {
        "x": np.ascontiguousarray(r_x),
        "x_t": np.ascontiguousarray(r_x.T),
        "w": np.ascontiguousarray(L0_rec_W),
        "b": np.ascontiguousarray(L0_rec_b).reshape(1, -1),
        "gamma": np.ascontiguousarray(L0_rec_gamma).reshape(1, -1),
        "beta": np.ascontiguousarray(L0_rec_beta).reshape(1, -1),
    }
    args = [nc.dram_tensor(name, a.shape, mybir.dt.from_np(a.dtype), kind="ExternalInput").ap() for name, a in arrays.items()]
    args.append(nc.dram_tensor("out", (BATCH, OUT), F32, kind="ExternalOutput").ap())
    build(nc, *args)
    result = run_bass_kernel_spmd(nc, [arrays], core_ids=[0])
    return result.results[0]["out"]
```

```python
from contextlib import ExitStack

import concourse.bass as bass
from concourse import mybir

F32 = mybir.dt.float32
F32R = mybir.dt.float32r
ALU = mybir.AluOpType
ACT = mybir.ActivationFunctionType
EPS = 1e-5

D, BATCH, OUT = 64, 512, 512
P = 128
BT = BATCH // P
PAIRS = D * (D - 1) // 2
TRIPLES = D * (D - 1) * (D - 2) // 6
TOTAL = D + PAIRS + TRIPLES
PT = -(-PAIRS // P)
LEAD = PT * P - PAIRS


def n_pairs(i):
    return (D - 1 - i) * (D - 2 - i) // 2


def first_pair(i):
    return PAIRS - (D - i) * (D - 1 - i) // 2


def first_triple(i):
    return TOTAL - (D - i) * (D - 1 - i) * (D - 2 - i) // 6


GROUPS = sum(n_pairs(i) >= P for i in range(D))
SEGMENTS = []
_tiles = 0
for _n in range(1, PT):
    _gs = [g for g in range(GROUPS) if n_pairs(GROUPS - 1 - g) // P == _n]
    SEGMENTS.append((_n, _gs[0], len(_gs), _tiles))
    _tiles += _n * len(_gs)
PAIR_TILE0 = _tiles
PACK_TILE0 = PAIR_TILE0 + PT

RUNS = [(0, D - LEAD, 0, None, None)]
_row = D - LEAD
for _i in range(D - 2):
    _rows = n_pairs(_i) % P
    if _rows:
        RUNS.append((_row, _rows, first_triple(_i), _i, LEAD + first_pair(_i + 1)))
        _row += _rows
PACKED = _row
PACKS = -(-PACKED // P)
LAST_ROWS = PACKED - (PACKS - 1) * P


def pieces(tile):
    out = []
    for at, rows, w, x, p in RUNS:
        lo, hi = max(at, tile * P), min(at + rows, (tile + 1) * P)
        if lo < hi:
            out.append((lo - tile * P, hi - lo, w + lo - at, x, None if p is None else p + lo - at))
    return out


def pair_runs(tile):
    out = []
    for j in range(D - 1):
        at = LEAD + first_pair(j)
        lo, hi = max(at, tile * P), min(at + D - 1 - j, (tile + 1) * P)
        if lo < hi:
            out.append((lo - tile * P, hi - lo, j, j + 1 + lo - at))
    return out


RING = 8
GATHER = 3
FSLOTS = 3
PACK_BATCH = PT
BATCHES = -(-PACKS // PACK_BATCH)
LAST = FSLOTS


def selections():
    import numpy as np
    sel = np.zeros((D, 2 * P), np.float32)
    for p0, rows, j, k in pair_runs(PT - 1):
        for r in range(rows):
            sel[j, p0 + r] = 1.0
            sel[k + r, P + p0 + r] = 1.0
    return sel


def build(nc, x, x_t, sel, w, b, gamma, beta, out):
    ctx = ExitStack()
    with ctx:
        def sb(name, shape, dt=F32):
            return ctx.enter_context(nc.sbuf_tensor(name, shape, dt))

        def sem(name):
            return ctx.enter_context(nc.semaphore(name))

        p_hi = sb("p_hi", [P, PT, BATCH], F32R)
        p_lo = sb("p_lo", [P, PT, BATCH], F32R)
        w_raw = sb("w_raw", [P, 2, PT, OUT])
        w_hi = sb("w_hi", [P, RING, OUT], F32R)
        w_lo = sb("w_lo", [P, RING, OUT], F32R)
        left = sb("left", [P, GATHER, BATCH])
        right = sb("right", [P, GATHER, BATCH])
        prod = sb("prod", [P, GATHER, BATCH])
        f_hi = sb("f_hi", [P, FSLOTS, BATCH], F32R)
        f_lo = sb("f_lo", [P, FSLOTS, BATCH], F32R)
        acc = sb("acc", [P, BT, OUT])
        x_col = sb("x_col", [P, BT, D])
        b_all = sb("b_all", [P, OUT])
        gamma_all = sb("gamma_all", [P, OUT])
        beta_all = sb("beta_all", [P, OUT])
        stats = sb("stats", [P, BT, 6])
        mean_var = sb("mean_var", [P, BT, 2])
        small = sb("small", [P, BT, 6])
        psum = ctx.enter_context(nc.psum_tensor("psum", [P, 2 * BT, OUT], F32))
        p_list = nc.dram_tensor("p_list", (PT * P, BATCH), F32, kind="Internal").ap()

        consts_in = sem("consts_in")
        start_in = [sem("start_in_x"), sem("start_in_sel")]
        selected = sem("selected")
        factor_copied = sem("factor_copied")
        gathered = [sem(f"gathered{s}") for s in range(GATHER)]
        packed_gathered = [sem(f"packed_gathered{s}") for s in range(GATHER)]
        norm_in = sem("norm_in")
        ones_set = sem("ones_set")
        prod_ready = sem("prod_ready")
        p_stored = sem("p_stored")
        feat_hi = sem("feat_hi")
        p_ready = sem("p_ready")
        f_ready = sem("f_ready")
        w_landed = sem("w_landed")
        pack_landed = [sem(f"pack_landed{s}") for s in range(BATCHES)]
        hi_ready = sem("hi_ready")
        lo_ready = sem("lo_ready")
        w_used = sem("w_used")
        drained = sem("drained")
        all_summed = [sem(f"all_summed{m}") for m in range(BT)]
        ln_step = sem("ln_step")
        veps_ready = sem("veps_ready")
        root_ready = sem("root_ready")
        normed = sem("normed")
        relu_done = sem("relu_done")
        stored = sem("stored")
        block = ctx.enter_context(nc.Block())

        def gather_dmas(f):
            s = f % GATHER
            first, second = [], []
            if f < PT:
                tile = PT - 1 - f
                if tile == 0:
                    first.append((left[0:LEAD, s, :], x_t[D - LEAD:D, :]))
                for p0, rows, j, k in pair_runs(tile):
                    first.append((left[p0:p0 + rows, s, :], x_t[j:j + 1, :].to_broadcast([rows, BATCH])))
                    second.append((right[p0:p0 + rows, s, :], x_t[k:k + rows, :]))
                return first, second
            for p0, rows, _, i, q in pieces(f - PT):
                if i is None:
                    first.append((left[p0:p0 + rows, s, :], x_t[0:rows, :]))
                else:
                    first.append((left[p0:p0 + rows, s, :], x_t[i:i + 1, :].to_broadcast([rows, BATCH])))
                    second.append((right[p0:p0 + rows, s, :], p_list[q:q + rows, :]))
            return first, second

        GATHER_DONE = [None]
        for f in range(1, PT + PACKS):
            signal = (gathered if f < PT else packed_gathered)[f % GATHER]
            earlier = max([v for s, v in GATHER_DONE[1:] if s is signal], default=0)
            GATHER_DONE.append((signal, earlier + 16 * sum(map(len, gather_dmas(f)))))
        ONES = {PT - 1: 1, PT: 2}

        def row_of_full(g, n):
            a = g + (D - GROUPS)
            return TOTAL - a * (a - 1) * (a - 2) // 6 - n * P

        def result(m):
            return (right, prod)[m // 2][:, m % 2, :]

        @block.sync
        def _(sp):
            def load(row, n, buf):
                src = w[bass.ds(row, n * P), :].rearrange("(t p) o -> p t o", p=P)
                sp.dma_start(w_raw[:, buf, 0:n, :], src).then_inc(w_landed, 16)

            sp.dma_start(left[0:D, 0, :], x_t).then_inc(start_in[0], 16)
            before = []
            for n, g0, count, k0 in SEGMENTS:
                before += [k0 + n * c for c in range(count)]
            for n, g0, count, k0 in SEGMENTS:
                peel = count if g0 == 0 else 1
                for g in range(g0, g0 + peel):
                    if g >= 1:
                        sp.wait_ge(w_landed, 16 * g)
                    if g >= 2:
                        sp.wait_ge(lo_ready, before[g - 1])
                    load(row_of_full(g, n), n, g % 2)
                if count > peel:
                    with sp.Fori(g0 + peel, g0 + count) as g:
                        sp.wait_ge(w_landed, g * 16)
                        sp.wait_ge(lo_ready, (g - (g0 + 1)) * n + k0)
                        load(row_of_full(g, n), n, g % 2)
            sp.wait_ge(w_landed, 16 * GROUPS)
            sp.wait_ge(lo_ready, before[GROUPS - 1])
            sp.dma_start(w_raw[:, GROUPS % 2, :, :], w[D - LEAD:D - LEAD + PT * P, :].rearrange("(t p) o -> p t o", p=P)).then_inc(w_landed, 16)
            sp.wait_ge(p_stored, 16 * PT)
            for f in range(PT, PT + PACKS):
                sp.wait_ge(prod_ready, f - GATHER + 1)
                for dst, src in gather_dmas(f)[1]:
                    sp.dma_start(dst, src).then_inc(GATHER_DONE[f][0], 16)
            for m in range(BT):
                sp.wait_ge(relu_done, m + 1)
                sp.dma_start(out[m * P:(m + 1) * P, :], result(m)).then_inc(stored, 16)
            sp.wait_ge(stored, 16 * BT)

        @block.gpsimd
        def _(pool):
            def ones(f, value):
                nc.gpsimd.memset(right[0:(LEAD if f < PT else D - LEAD), f % GATHER, :], 1.0).then_inc(ones_set, 1)

            def gather(f):
                if f >= GATHER:
                    pool.wait_ge(prod_ready, f - GATHER + 1)
                if f in ONES:
                    ones(f, 1.0)
                for dst, src in sum(gather_dmas(f), []) if f < PT else []:
                    pool.dma_start(dst, src).then_inc(GATHER_DONE[f][0], 16)

            def store(f):
                tile = PT - 1 - f
                pool.wait_ge(prod_ready, f + 1)
                if f:
                    pool.wait_ge(p_stored, 16 * f)
                pool.dma_start(p_list[tile * P:(tile + 1) * P, :], prod[:, f % GATHER, :]).then_inc(p_stored, 16)

            gather(1)
            for f in range(2, PT):
                gather(f)
                store(f - 2)
            pool.dma_start(gamma_all[:], gamma.to_broadcast([P, OUT])).then_inc(norm_in, 16)
            pool.dma_start(beta_all[:], beta.to_broadcast([P, OUT])).then_inc(norm_in, 16)
            for f in range(PT - 2, PT):
                store(f)
            gather(PT)
            for batch in range(BATCHES):
                pool.wait_ge(lo_ready, PAIR_TILE0 + PT * batch)
                for tile in range(PACK_BATCH * batch, min(PACKS, PACK_BATCH * (batch + 1))):
                    for p0, rows, row, _, _ in pieces(tile):
                        pool.dma_start(w_raw[p0:p0 + rows, (GROUPS + 1 + batch) % 2, tile % PACK_BATCH, :],
                                     w[row:row + rows, :]).then_inc(pack_landed[batch], 16)

        @block.scalar
        def _(act):
            def split_hi(raw, k, rows=P):
                act.wait_ge(w_used, k + 1)
                nc.scalar.copy(w_hi[0:rows, k % RING, :], raw).then_inc(hi_ready, 1)

            act.dma_start(right[0:D, 0, 0:2 * P], sel).then_inc(start_in[1], 16)
            act.dma_start(x_col[:], x.rearrange("(m p) d -> p m d", p=P)).then_inc(consts_in, 16)
            act.dma_start(b_all[:], b.to_broadcast([P, OUT])).then_inc(consts_in, 16)
            act.wait_ge(selected, 1)
            nc.scalar.copy(right[:, 0, :], psum[:, BT + 1, :]).then_inc(factor_copied, 1)

            for n, g0, count, k0 in SEGMENTS:
                with act.Fori(g0, g0 + count) as g:
                    act.wait_ge(w_landed, g * 16 + 16)
                    for t in range(n):
                        split_hi(w_raw[:, g % 2, t, :], (g - g0) * n + (k0 + t))
            act.wait_ge(w_landed, 16 * (GROUPS + 1))

            def gather_left(f):
                act.wait_ge(prod_ready, f - GATHER + 1)
                for dst, src in gather_dmas(f)[0]:
                    act.dma_start(dst, src).then_inc(GATHER_DONE[f][0], 16)

            for t in range(PT):
                if t in (PT - 3, PT - 2, PT - 1):
                    gather_left(PT + t - (PT - 3))
                split_hi(w_raw[:, GROUPS % 2, t, :], PAIR_TILE0 + t)
            for batch in range(BATCHES):
                tiles = range(PACK_BATCH * batch, min(PACKS, PACK_BATCH * (batch + 1)))
                act.wait_ge(pack_landed[batch], 16 * sum(len(pieces(t)) for t in tiles))
                for tile in tiles:
                    rows = P if tile < PACKS - 1 else LAST_ROWS
                    split_hi(w_raw[0:rows, (GROUPS + 1 + batch) % 2, tile % PACK_BATCH, :], PACK_TILE0 + tile, rows)
                    if 1 <= tile <= PACKS - GATHER:
                        gather_left(PT + tile + GATHER - 1)
            for m in range(BT):
                act.wait_ge(veps_ready, m + 1)
                nc.scalar.activation(small[:, m, 1:2], small[:, m, 0:1], ACT.Sqrt).then_inc(root_ready, 1)
                act.wait_ge(normed, m + 1)
                o = result(m)
                nc.scalar.activation(o, o, ACT.Relu).then_inc(relu_done, 1)

        @block.vector
        def _(dve):
            dve.sem_inc(drained, 2 * BT)

            steps = [0]

            def after(ins):
                steps[0] += 1
                ins.then_inc(ln_step, 1)
                dve.wait_ge(ln_step, steps[0])

            def split_lo(raw, k, rows=P):
                dve.wait_ge(hi_ready, k + 1)
                nc.vector.tensor_tensor(w_lo[0:rows, k % RING, :], raw, w_hi[0:rows, k % RING, :].bitcast(F32),
                                        ALU.subtract).then_inc(lo_ready, 1)

            def multiply(f, rows=P):
                s = f % GATHER
                if f:
                    dve.wait_ge(*GATHER_DONE[f])
                else:
                    dve.wait_ge(factor_copied, 1)
                if f in ONES:
                    dve.wait_ge(ones_set, ONES[f])
                if GATHER <= f < PT + GATHER:
                    dve.wait_ge(p_stored, 16 * (f - GATHER + 1))
                if f >= GATHER:
                    dve.wait_ge(prod_ready, f - GATHER + 1)
                nc.vector.tensor_tensor(prod[0:rows, s, :], left[0:rows, s, :] if f else psum[:, BT, :], right[0:rows, s, :], ALU.mult).then_inc(prod_ready, 1)
                dve.wait_ge(prod_ready, f + 1)

            def split(f, hi, lo, ready, rows=P):
                s = f % GATHER
                nc.vector.tensor_copy(hi, prod[0:rows, s, :]).then_inc(feat_hi, 1)
                dve.wait_ge(feat_hi, f + 1)
                nc.vector.tensor_tensor(lo, prod[0:rows, s, :], hi.bitcast(F32), ALU.subtract).then_inc(ready, 1)

            def build_p(f):
                tile = PT - 1 - f
                multiply(f)
                split(f, p_hi[:, tile, :], p_lo[:, tile, :], p_ready)

            def drain(g, tiles, first=False):
                dve.wait_ge(w_used, tiles + RING)
                for m in range(BT):
                    if not first:
                        dve.wait_ge(drained, g * BT + (BT + m + 1))
                    nc.vector.scalar_tensor_tensor(
                        out=acc[:, m, :], in0=psum[:, (g % 2) * BT + m, :], scalar=x_col[:, m, bass.ds((GROUPS - 1) - g, 1)],
                        in1=b_all[:] if first else acc[:, m, :], op0=ALU.mult, op1=ALU.add).then_inc(drained, 1)

            def lo_of_group(g, n, g0, k0):
                for t in range(n):
                    split_lo(w_raw[:, g % 2, t, :], (g - g0) * n + (k0 + t))

            build_p(0)
            for n, g0, count, k0 in SEGMENTS:
                peel = 2 if g0 == 0 else 0
                if peel:
                    lo_of_group(0, n, g0, k0)
                    lo_of_group(1, n, g0, k0)
                    dve.wait_ge(consts_in, 32)
                    drain(0, 1, first=True)
                with dve.Fori(g0 + peel, g0 + count) as g:
                    lo_of_group(g, n, g0, k0)
                    drain(g - 1, (g - g0) * n + k0)
                build_p(n)
            def packed_lo(tile):
                rows = P if tile < PACKS - 1 else LAST_ROWS
                split_lo(w_raw[0:rows, (GROUPS + 1 + tile // PACK_BATCH) % 2, tile % PACK_BATCH, :], PACK_TILE0 + tile, rows)

            def packed_feature(tile):
                rows = P if tile < PACKS - 1 else LAST_ROWS
                f, s = PT + tile, tile % FSLOTS
                multiply(f, rows)
                if tile >= FSLOTS:
                    dve.wait_ge(w_used, RING + PACK_TILE0 + tile - FSLOTS + 1)
                split(f, f_hi[0:rows, s, :], f_lo[0:rows, s, :], f_ready, rows)

            for t in range(PT):
                split_lo(w_raw[:, GROUPS % 2, t, :], PAIR_TILE0 + t)
                if t == 0:
                    drain(GROUPS - 1, PAIR_TILE0)
            for tile in range(FSLOTS - 1):
                packed_feature(tile)
                packed_lo(tile)
            for tile in range(FSLOTS - 1, PACKS):
                packed_lo(tile)
                packed_feature(tile)

            dve.wait_ge(norm_in, 32)
            dve.wait_ge(prod_ready, PT + PACKS)
            for m in range(BT):
                dve.wait_ge(all_summed[m], 1)
                h = acc[:, m, :]
                o = result(m)
                veps, root, y, yy, c, rstd = (small[:, m, c:c + 1] for c in range(6))
                dve.wait_ge(drained, (GROUPS + 1) * BT + m + 1)
                after(nc.vector.tensor_tensor(h, psum[:, (GROUPS % 2) * BT + m, :], h, ALU.add))
                after(nc.vector.bn_stats(stats[:, m, :], h))
                after(nc.vector.bn_aggr(mean_var[:, m, :], stats[:, m, :]))
                nc.vector.tensor_scalar(veps, mean_var[:, m, 1:2], EPS, None, ALU.add).then_inc(veps_ready, 1)
                after(nc.vector.scalar_tensor_tensor(out=o, in0=h, scalar=mean_var[:, m, 0:1], in1=gamma_all[:], op0=ALU.subtract, op1=ALU.mult))
                dve.wait_ge(root_ready, m + 1)
                after(nc.vector.reciprocal(y, root))
                after(nc.vector.scalar_tensor_tensor(out=yy, in0=y, scalar=veps, in1=y, op0=ALU.mult, op1=ALU.mult))
                after(nc.vector.tensor_scalar(c, yy, -0.5, 1.5, ALU.mult, ALU.add))
                after(nc.vector.tensor_tensor(rstd, y, c, ALU.mult))
                nc.vector.scalar_tensor_tensor(out=o, in0=o, scalar=rstd, in1=beta_all[:], op0=ALU.mult, op1=ALU.add).then_inc(normed, 1)

        @block.tensor
        def _(pe):
            pe.sem_inc(w_used, RING)

            pe.wait_ge(start_in[0], 16)
            pe.wait_ge(start_in[1], 16)
            for c in range(2):
                last = nc.tensor.matmul(psum[:, BT + c, :], right[0:D, 0, c * P:(c + 1) * P], left[0:D, 0, :], start=True, stop=True)
            last.then_inc(selected, 1)

            def k_tile(hi, lo, k, bank, start, stop, rows=P, batch_tiles=range(BT)):
                wh = w_hi[0:rows, k % RING, :]
                wl = w_lo[0:rows, k % RING, :]
                for m in batch_tiles:
                    cols = slice(m * P, (m + 1) * P)
                    nc.tensor.matmul(psum[:, bank + m, :], hi[:, cols], wh, start=start, stop=False)
                    nc.tensor.matmul(psum[:, bank + m, :], hi[:, cols], wl, start=False, stop=False)
                    last = nc.tensor.matmul(psum[:, bank + m, :], lo[:, cols], wh, start=False, stop=stop)
                return last

            for n, g0, count, k0 in SEGMENTS:
                pe.wait_ge(p_ready, n)
                with pe.Fori(g0, g0 + count) as g:
                    pe.wait_ge(drained, g * BT + BT)
                    for t in range(n):
                        k = (g - g0) * n + (k0 + t)
                        pe.wait_ge(lo_ready, k + 1)
                        last = k_tile(p_hi[:, PT - n + t, :], p_lo[:, PT - n + t, :], k, (g % 2) * BT, t == 0, t == n - 1)
                        last.then_inc(w_used, 1)
            bank = (GROUPS % 2) * BT
            pe.wait_ge(p_ready, PT)
            pe.wait_ge(drained, (GROUPS + 1) * BT)
            for t in range(PT):
                pe.wait_ge(lo_ready, PAIR_TILE0 + t + 1)
                k_tile(p_hi[:, t, :], p_lo[:, t, :], PAIR_TILE0 + t, bank, t == 0, False).then_inc(w_used, 1)
            for tile in range(PACKS - LAST):
                pe.wait_ge(f_ready, tile + 1)
                pe.wait_ge(lo_ready, PACK_TILE0 + tile + 1)
                k_tile(f_hi[:, tile % FSLOTS, :], f_lo[:, tile % FSLOTS, :], PACK_TILE0 + tile, bank, False, False).then_inc(w_used, 1)
            for m in range(BT):
                for tile in range(PACKS - LAST, PACKS):
                    rows = P if tile < PACKS - 1 else LAST_ROWS
                    if m == 0:
                        pe.wait_ge(f_ready, tile + 1)
                        pe.wait_ge(lo_ready, PACK_TILE0 + tile + 1)
                    last = k_tile(f_hi[0:rows, tile % FSLOTS, :], f_lo[0:rows, tile % FSLOTS, :], PACK_TILE0 + tile, bank,
                                  False, tile == PACKS - 1, rows, [m])
                last.then_inc(all_summed[m], 1)


def kernel(r_x, L0_rec_W, L0_rec_b, L0_rec_gamma, L0_rec_beta):
    import concourse.bacc as bacc
    import numpy as np
    from concourse.bass_utils import run_bass_kernel_spmd

    nc = bacc.Bacc("TRN2", target_bir_lowering=False, num_devices=1)
    r_x = np.asarray(r_x)
    arrays = {
        "x": np.ascontiguousarray(r_x),
        "x_t": np.ascontiguousarray(r_x.T),
        "sel": selections(),
        "w": np.ascontiguousarray(L0_rec_W),
        "b": np.ascontiguousarray(L0_rec_b).reshape(1, -1),
        "gamma": np.ascontiguousarray(L0_rec_gamma).reshape(1, -1),
        "beta": np.ascontiguousarray(L0_rec_beta).reshape(1, -1),
    }
    args = [nc.dram_tensor(name, a.shape, mybir.dt.from_np(a.dtype), kind="ExternalInput").ap() for name, a in arrays.items()]
    args.append(nc.dram_tensor("out", (BATCH, OUT), F32, kind="ExternalOutput").ap())
    build(nc, *args)
    result = run_bass_kernel_spmd(nc, [arrays], core_ids=[0])
    return result.results[0]["out"]
```

```python
from contextlib import ExitStack

import concourse.bass as bass
from concourse import mybir

F32 = mybir.dt.float32
F32R = mybir.dt.float32r
ALU = mybir.AluOpType
ACT = mybir.ActivationFunctionType
EPS = 1e-5

D, BATCH, OUT = 64, 512, 512
P = 128
BT = BATCH // P
PAIRS = D * (D - 1) // 2
TRIPLES = D * (D - 1) * (D - 2) // 6
TOTAL = D + PAIRS + TRIPLES
PT = -(-PAIRS // P)
LEAD = PT * P - PAIRS


def n_pairs(i):
    return (D - 1 - i) * (D - 2 - i) // 2


def first_pair(i):
    return PAIRS - (D - i) * (D - 1 - i) // 2


def first_triple(i):
    return TOTAL - (D - i) * (D - 1 - i) * (D - 2 - i) // 6


MIN_TILES = 2

GROUPS = sum(n_pairs(i) >= MIN_TILES * P for i in range(D))
SEGMENTS = []
_tiles = 0
for _n in range(MIN_TILES, PT):
    _gs = [g for g in range(GROUPS) if n_pairs(GROUPS - 1 - g) // P == _n]
    SEGMENTS.append((_n, _gs[0], len(_gs), _tiles))
    _tiles += _n * len(_gs)
PAIR_TILE0 = _tiles
PACK_TILE0 = PAIR_TILE0 + PT

RUNS = [(0, D - LEAD, 0, None, None)]
_row = D - LEAD
for _i in range(D - 2):
    _rows = n_pairs(_i) % P if _i < GROUPS else n_pairs(_i)
    if _rows:
        RUNS.append((_row, _rows, first_triple(_i), _i, LEAD + first_pair(_i + 1)))
        _row += _rows
PACKED = _row
PACKS = -(-PACKED // P)
LAST_ROWS = PACKED - (PACKS - 1) * P


def pieces(tile):
    out = []
    for at, rows, w, x, p in RUNS:
        lo, hi = max(at, tile * P), min(at + rows, (tile + 1) * P)
        if lo < hi:
            out.append((lo - tile * P, hi - lo, w + lo - at, x, None if p is None else p + lo - at))
    return out


def pair_runs(tile):
    out = []
    for j in range(D - 1):
        at = LEAD + first_pair(j)
        lo, hi = max(at, tile * P), min(at + D - 1 - j, (tile + 1) * P)
        if lo < hi:
            out.append((lo - tile * P, hi - lo, j, j + 1 + lo - at))
    return out


RING = 8
GATHER = 4
FSLOTS = 8
SELECTED = MIN_TILES
PACK_BATCH = PT
BATCHES = -(-PACKS // PACK_BATCH)
LAST = 6


def feature_at(tile):
    return tile + RING if tile < FSLOTS else PT + tile


def selections():
    import numpy as np
    sel = np.zeros((D, SELECTED * 2 * P), np.float32)
    for f in range(SELECTED):
        for p0, rows, j, k in pair_runs(PT - 1 - f):
            for r in range(rows):
                sel[j, f * 2 * P + p0 + r] = 1.0
                sel[k + r, f * 2 * P + P + p0 + r] = 1.0
    return sel


def build(nc, x, x_t, sel, w, b, gamma, beta, out):
    ctx = ExitStack()
    with ctx:
        def sb(name, shape, dt=F32):
            return ctx.enter_context(nc.sbuf_tensor(name, shape, dt))

        def sem(name):
            return ctx.enter_context(nc.semaphore(name))

        p_hi = sb("p_hi", [P, PT, BATCH], F32R)
        p_lo = sb("p_lo", [P, PT, BATCH], F32R)
        w_raw = sb("w_raw", [P, 2, PT, OUT])
        w_hi = sb("w_hi", [P, RING, OUT], F32R)
        w_lo = sb("w_lo", [P, RING, OUT], F32R)
        left = sb("left", [P, GATHER, BATCH])
        right = sb("right", [P, GATHER, BATCH])
        prod = sb("prod", [P, GATHER, BATCH])
        acc = sb("acc", [P, BT, OUT])
        x_col = sb("x_col", [P, BT, D])
        b_all = sb("b_all", [P, OUT])
        gamma_all = sb("gamma_all", [P, OUT])
        beta_all = sb("beta_all", [P, OUT])
        stats = sb("stats", [P, BT, 6])
        mean_var = sb("mean_var", [P, BT, 2])
        small = sb("small", [P, BT, 6])
        psum = ctx.enter_context(nc.psum_tensor("psum", [P, 2 * BT, OUT], F32))
        p_list = nc.dram_tensor("p_list", (PT * P, BATCH), F32, kind="Internal").ap()

        consts_in = sem("consts_in")
        start_in = [sem("start_in_x"), sem("start_in_sel")]
        selected = sem("selected")
        factor_copied = sem("factor_copied")
        gathered = [sem(f"gathered{s}") for s in range(GATHER)]
        packed_gathered = [sem(f"packed_gathered{s}") for s in range(GATHER)]
        norm_in = sem("norm_in")
        ones_set = sem("ones_set")
        prod_ready = sem("prod_ready")
        p_stored = sem("p_stored")
        feat_hi = sem("feat_hi")
        p_ready = sem("p_ready")
        f_ready = sem("f_ready")
        w_landed = sem("w_landed")
        pack_landed = [sem(f"pack_landed{s}") for s in range(BATCHES)]
        hi_ready = sem("hi_ready")
        lo_ready = sem("lo_ready")
        w_used = sem("w_used")
        drained = sem("drained")
        all_summed = [sem(f"all_summed{m}") for m in range(BT)]
        ln_step = sem("ln_step")
        veps_ready = sem("veps_ready")
        root_ready = sem("root_ready")
        normed = sem("normed")
        relu_done = sem("relu_done")
        stored = sem("stored")
        block = ctx.enter_context(nc.Block())

        def gather_dmas(f):
            s = f % GATHER
            first, second = [], []
            if f < PT:
                tile = PT - 1 - f
                if tile == 0:
                    first.append((left[0:LEAD, s, :], x_t[D - LEAD:D, :]))
                for p0, rows, j, k in pair_runs(tile):
                    first.append((left[p0:p0 + rows, s, :], x_t[j:j + 1, :].to_broadcast([rows, BATCH])))
                    second.append((right[p0:p0 + rows, s, :], x_t[k:k + rows, :]))
                return first, second
            for p0, rows, _, i, q in pieces(f - PT):
                if i is None:
                    first.append((left[p0:p0 + rows, s, :], x_t[0:rows, :]))
                else:
                    first.append((left[p0:p0 + rows, s, :], x_t[i:i + 1, :].to_broadcast([rows, BATCH])))
                    second.append((right[p0:p0 + rows, s, :], p_list[q:q + rows, :]))
            return first, second

        GATHER_DONE = [None] * SELECTED
        for f in range(SELECTED, PT + PACKS):
            signal = (gathered if f < PT else packed_gathered)[f % GATHER]
            earlier = max([v for s, v in GATHER_DONE[SELECTED:] if s is signal], default=0)
            GATHER_DONE.append((signal, earlier + 16 * sum(map(len, gather_dmas(f)))))
        ONES = {PT - 1: 1, PT: 2}

        def row_of_full(g, n):
            a = g + (D - GROUPS)
            return TOTAL - a * (a - 1) * (a - 2) // 6 - n * P

        def result(m):
            return (right, prod)[m // 2][:, m % 2, :]

        @block.sync
        def _(sp):
            def load(row, n, buf):
                src = w[bass.ds(row, n * P), :].rearrange("(t p) o -> p t o", p=P)
                sp.dma_start(w_raw[:, buf, 0:n, :], src).then_inc(w_landed, 16)

            sp.dma_start(left[0:D, SELECTED, :], x_t).then_inc(start_in[0], 16)
            before = []
            for n, g0, count, k0 in SEGMENTS:
                before += [k0 + n * c for c in range(count)]
            for n, g0, count, k0 in SEGMENTS:
                peel = 2 if g0 == 0 else 1
                for g in range(g0, g0 + peel):
                    if g >= 1:
                        sp.wait_ge(w_landed, 16 * g)
                    if g >= 2:
                        sp.wait_ge(lo_ready, before[g - 1])
                    load(row_of_full(g, n), n, g % 2)
                if count > peel:
                    with sp.Fori(g0 + peel, g0 + count) as g:
                        sp.wait_ge(w_landed, g * 16)
                        sp.wait_ge(lo_ready, (g - (g0 + 1)) * n + k0)
                        load(row_of_full(g, n), n, g % 2)
            sp.wait_ge(w_landed, 16 * GROUPS)
            sp.wait_ge(lo_ready, before[GROUPS - 1])
            sp.dma_start(w_raw[:, GROUPS % 2, :, :],
                         w[D - LEAD:D - LEAD + PT * P, :].rearrange("(t p) o -> p t o", p=P)).then_inc(w_landed, 16)
            sp.wait_ge(p_stored, 16 * PT)
            for f in range(PT, PT + PACKS):
                sp.wait_ge(prod_ready, f - GATHER + 1)
                for dst, src in gather_dmas(f)[1]:
                    sp.dma_start(dst, src).then_inc(GATHER_DONE[f][0], 16)
            for m in range(BT):
                sp.wait_ge(relu_done, m + 1)
                sp.dma_start(out[m * P:(m + 1) * P, :], result(m)).then_inc(stored, 16)
            sp.wait_ge(stored, 16 * BT)

        @block.gpsimd
        def _(pool):
            def gather(f):
                if f == SELECTED:
                    pool.wait_ge(selected, SELECTED)
                if f >= GATHER:
                    pool.wait_ge(prod_ready, f - GATHER + 1)
                if f in ONES:
                    nc.gpsimd.memset(right[0:(LEAD if f < PT else D - LEAD), f % GATHER, :], 1.0).then_inc(ones_set, 1)
                for dst, src in sum(gather_dmas(f), []) if f < PT else []:
                    pool.dma_start(dst, src).then_inc(GATHER_DONE[f][0], 16)

            def store(f):
                tile = PT - 1 - f
                pool.wait_ge(prod_ready, f + 1)
                if f:
                    pool.wait_ge(p_stored, 16 * f)
                pool.dma_start(p_list[tile * P:(tile + 1) * P, :], prod[:, f % GATHER, :]).then_inc(p_stored, 16)

            for f in range(SELECTED, PT):
                gather(f)
                store(f - 2)
            pool.dma_start(gamma_all[:], gamma.to_broadcast([P, OUT])).then_inc(norm_in, 16)
            pool.dma_start(beta_all[:], beta.to_broadcast([P, OUT])).then_inc(norm_in, 16)
            for f in range(PT - 2, PT):
                store(f)
            gather(PT)
            for batch in range(BATCHES):
                pool.wait_ge(lo_ready, PAIR_TILE0 + PT * batch)
                for tile in range(PACK_BATCH * batch, min(PACKS, PACK_BATCH * (batch + 1))):
                    for p0, rows, row, _, _ in pieces(tile):
                        pool.dma_start(w_raw[p0:p0 + rows, (GROUPS + 1 + batch) % 2, tile % PACK_BATCH, :],
                                       w[row:row + rows, :]).then_inc(pack_landed[batch], 16)

        @block.scalar
        def _(act):
            def split_hi(raw, k, rows=P):
                act.wait_ge(w_used, k + 1)
                nc.scalar.copy(w_hi[0:rows, k % RING, :], raw).then_inc(hi_ready, 1)

            act.dma_start(right[0:D, SELECTED, 0:SELECTED * 2 * P], sel).then_inc(start_in[1], 16)
            act.dma_start(x_col[:], x.rearrange("(m p) d -> p m d", p=P)).then_inc(consts_in, 16)
            act.dma_start(b_all[:], b.to_broadcast([P, OUT])).then_inc(consts_in, 16)

            def hi_of_group(g, n, g0, k0):
                act.wait_ge(w_landed, g * 16 + 16)
                for t in range(n):
                    split_hi(w_raw[:, g % 2, n - 1 - t, :], (g - g0) * n + (k0 + t))

            hi_of_group(0, *SEGMENTS[0][:2], 0)
            for f in range(SELECTED):
                act.wait_ge(selected, f + 1)
                nc.scalar.copy(right[:, f, :], psum[:, BT + 2 * f + 1, :]).then_inc(factor_copied, 1)

            for n, g0, count, k0 in SEGMENTS:
                peel = 1 if g0 == 0 else 0
                with act.Fori(g0 + peel, g0 + count) as g:
                    hi_of_group(g, n, g0, k0)
            act.wait_ge(w_landed, 16 * (GROUPS + 1))

            def gather_left(f):
                act.wait_ge(prod_ready, f - GATHER + 1)
                for dst, src in gather_dmas(f)[0]:
                    act.dma_start(dst, src).then_inc(GATHER_DONE[f][0], 16)

            def gather_lefts(at):
                for j in range(PACKS):
                    if at == (0 if j < GATHER else feature_at(j - GATHER) + 1):
                        gather_left(PT + j)

            for t in range(PT):
                split_hi(w_raw[:, GROUPS % 2, t, :], PAIR_TILE0 + t)
                gather_lefts(t)
            for batch in range(BATCHES):
                tiles = range(PACK_BATCH * batch, min(PACKS, PACK_BATCH * (batch + 1)))
                act.wait_ge(pack_landed[batch], 16 * sum(len(pieces(t)) for t in tiles))
                for tile in tiles:
                    rows = P if tile < PACKS - 1 else LAST_ROWS
                    split_hi(w_raw[0:rows, (GROUPS + 1 + batch) % 2, tile % PACK_BATCH, :], PACK_TILE0 + tile, rows)
                    gather_lefts(PT + tile)
            for m in range(BT):
                act.wait_ge(veps_ready, m + 1)
                nc.scalar.activation(small[:, m, 1:2], small[:, m, 0:1], ACT.Sqrt).then_inc(root_ready, 1)
                act.wait_ge(normed, m + 1)
                o = result(m)
                nc.scalar.activation(o, o, ACT.Relu).then_inc(relu_done, 1)

        @block.vector
        def _(dve):
            dve.sem_inc(drained, 2 * BT)

            steps = [0]

            def after(ins):
                steps[0] += 1
                ins.then_inc(ln_step, 1)
                dve.wait_ge(ln_step, steps[0])

            def split_lo(raw, k, rows=P):
                dve.wait_ge(hi_ready, k + 1)
                nc.vector.tensor_tensor(w_lo[0:rows, k % RING, :], raw, w_hi[0:rows, k % RING, :].bitcast(F32),
                                        ALU.subtract).then_inc(lo_ready, 1)

            def multiply(f, rows=P):
                s = f % GATHER
                if f >= SELECTED:
                    dve.wait_ge(*GATHER_DONE[f])
                else:
                    dve.wait_ge(factor_copied, f + 1)
                if f in ONES:
                    dve.wait_ge(ones_set, ONES[f])
                if GATHER <= f < PT + GATHER:
                    dve.wait_ge(p_stored, 16 * (f - GATHER + 1))
                if f >= GATHER:
                    dve.wait_ge(prod_ready, f - GATHER + 1)
                first = left[0:rows, s, :] if f >= SELECTED else psum[:, BT + 2 * f, :]
                nc.vector.tensor_tensor(prod[0:rows, s, :], first, right[0:rows, s, :], ALU.mult).then_inc(prod_ready, 1)
                dve.wait_ge(prod_ready, f + 1)

            def split(f, hi, lo, ready, rows=P):
                s = f % GATHER
                nc.vector.tensor_copy(hi, prod[0:rows, s, :]).then_inc(feat_hi, 1)
                dve.wait_ge(feat_hi, f + 1)
                nc.vector.tensor_tensor(lo, prod[0:rows, s, :], hi.bitcast(F32), ALU.subtract).then_inc(ready, 1)

            def build_p(f):
                tile = PT - 1 - f
                multiply(f)
                split(f, p_hi[:, tile, :], p_lo[:, tile, :], p_ready)

            def drain(g, tiles, first=False):
                dve.wait_ge(w_used, tiles + RING)
                for m in range(BT):
                    if not first:
                        dve.wait_ge(drained, g * BT + (BT + m + 1))
                    nc.vector.scalar_tensor_tensor(
                        out=acc[:, m, :], in0=psum[:, (g % 2) * BT + m, :], scalar=x_col[:, m, bass.ds((GROUPS - 1) - g, 1)],
                        in1=b_all[:] if first else acc[:, m, :], op0=ALU.mult, op1=ALU.add).then_inc(drained, 1)

            def lo_of_group(g, n, g0, k0):
                for t in range(n):
                    split_lo(w_raw[:, g % 2, n - 1 - t, :], (g - g0) * n + (k0 + t))

            lo_of_group(0, *SEGMENTS[0][:2], 0)
            for f in range(SELECTED):
                build_p(f)
            for n, g0, count, k0 in SEGMENTS:
                peel = 2 if g0 == 0 else 0
                if peel:
                    lo_of_group(1, n, g0, k0)
                    dve.wait_ge(consts_in, 32)
                    drain(0, n, first=True)
                with dve.Fori(g0 + peel, g0 + count) as g:
                    lo_of_group(g, n, g0, k0)
                    drain(g - 1, (g - g0) * n + k0)
                build_p(n)

            def packed_lo(tile):
                rows = P if tile < PACKS - 1 else LAST_ROWS
                split_lo(w_raw[0:rows, (GROUPS + 1 + tile // PACK_BATCH) % 2, tile % PACK_BATCH, :], PACK_TILE0 + tile, rows)

            def packed_feature(tile):
                rows = P if tile < PACKS - 1 else LAST_ROWS
                f, s = PT + tile, tile % FSLOTS
                multiply(f, rows)
                dve.wait_ge(w_used, RING + (PAIR_TILE0 if tile < FSLOTS else PACK_TILE0 - FSLOTS) + tile + 1)
                split(f, p_hi[0:rows, s, :], p_lo[0:rows, s, :], f_ready, rows)

            for t in range(PT):
                split_lo(w_raw[:, GROUPS % 2, t, :], PAIR_TILE0 + t)
                if t == 0:
                    drain(GROUPS - 1, PAIR_TILE0)
                for tile in range(FSLOTS):
                    if feature_at(tile) == t:
                        packed_feature(tile)
            for tile in range(PACKS):
                packed_lo(tile)
                if tile >= FSLOTS:
                    packed_feature(tile)

            dve.wait_ge(norm_in, 32)
            dve.wait_ge(prod_ready, PT + PACKS)
            for m in range(BT):
                dve.wait_ge(all_summed[m], 1)
                h = acc[:, m, :]
                o = result(m)
                veps, root, y, yy, c, rstd = (small[:, m, c:c + 1] for c in range(6))
                dve.wait_ge(drained, (GROUPS + 1) * BT + m + 1)
                after(nc.vector.tensor_tensor(h, psum[:, (GROUPS % 2) * BT + m, :], h, ALU.add))
                after(nc.vector.bn_stats(stats[:, m, :], h))
                after(nc.vector.bn_aggr(mean_var[:, m, :], stats[:, m, :]))
                nc.vector.tensor_scalar(veps, mean_var[:, m, 1:2], EPS, None, ALU.add).then_inc(veps_ready, 1)
                after(nc.vector.scalar_tensor_tensor(out=o, in0=h, scalar=mean_var[:, m, 0:1], in1=gamma_all[:],
                                                     op0=ALU.subtract, op1=ALU.mult))
                dve.wait_ge(root_ready, m + 1)
                after(nc.vector.reciprocal(y, root))
                after(nc.vector.scalar_tensor_tensor(out=yy, in0=y, scalar=veps, in1=y, op0=ALU.mult, op1=ALU.mult))
                after(nc.vector.tensor_scalar(c, yy, -0.5, 1.5, ALU.mult, ALU.add))
                after(nc.vector.tensor_tensor(rstd, y, c, ALU.mult))
                nc.vector.scalar_tensor_tensor(out=o, in0=o, scalar=rstd, in1=beta_all[:],
                                               op0=ALU.mult, op1=ALU.add).then_inc(normed, 1)

        @block.tensor
        def _(pe):
            assert FSLOTS % RING == 0
            pe.sem_inc(w_used, RING)

            pe.wait_ge(start_in[0], 16)
            pe.wait_ge(start_in[1], 16)
            for c in range(2 * SELECTED):
                last = nc.tensor.matmul(psum[:, BT + c, :], right[0:D, SELECTED, c * P:(c + 1) * P], left[0:D, SELECTED, :],
                                        start=True, stop=True)
                if c % 2:
                    last.then_inc(selected, 1)

            def k_tile(hi, lo, k, bank, start, stop, rows=P, batch_tiles=range(BT)):
                wh = w_hi[0:rows, k % RING, :]
                wl = w_lo[0:rows, k % RING, :]
                for m in batch_tiles:
                    cols = slice(m * P, (m + 1) * P)
                    nc.tensor.matmul(psum[:, bank + m, :], hi[:, cols], wh, start=start, stop=False)
                    nc.tensor.matmul(psum[:, bank + m, :], hi[:, cols], wl, start=False, stop=False)
                    last = nc.tensor.matmul(psum[:, bank + m, :], lo[:, cols], wh, start=False, stop=stop)
                return last

            for n, g0, count, k0 in SEGMENTS:
                with pe.Fori(g0, g0 + count) as g:
                    pe.wait_ge(drained, g * BT + BT)
                    for t in range(n):
                        k = (g - g0) * n + (k0 + t)
                        if n == MIN_TILES or t == n - 1:
                            pe.wait_ge(p_ready, t + 1)
                        pe.wait_ge(lo_ready, k + 1)
                        last = k_tile(p_hi[:, PT - 1 - t, :], p_lo[:, PT - 1 - t, :], k, (g % 2) * BT, t == 0, t == n - 1)
                        last.then_inc(w_used, 1)
            bank = (GROUPS % 2) * BT
            pe.wait_ge(p_ready, PT)
            pe.wait_ge(drained, (GROUPS + 1) * BT)
            for t in range(PT):
                pe.wait_ge(lo_ready, PAIR_TILE0 + t + 1)
                k_tile(p_hi[:, t, :], p_lo[:, t, :], PAIR_TILE0 + t, bank, t == 0, False).then_inc(w_used, 1)

            def packed(tile, at):
                pe.wait_ge(f_ready, tile + 1)
                pe.wait_ge(lo_ready, tile + (PACK_TILE0 + 1))
                k_tile(p_hi[:, at % FSLOTS, :], p_lo[:, at % FSLOTS, :], PACK_TILE0 + at, bank, False, False).then_inc(w_used, 1)

            rounds = (PACKS - LAST) // FSLOTS
            with pe.Fori(0, rounds * FSLOTS, FSLOTS) as tile:
                for at in range(FSLOTS):
                    packed(tile + at, at)
            for tile in range(rounds * FSLOTS, PACKS - LAST):
                packed(tile, tile)
            for m in range(BT):
                for tile in range(PACKS - LAST, PACKS):
                    rows = P if tile < PACKS - 1 else LAST_ROWS
                    if m == 0:
                        pe.wait_ge(f_ready, tile + 1)
                        pe.wait_ge(lo_ready, PACK_TILE0 + tile + 1)
                    last = k_tile(p_hi[0:rows, tile % FSLOTS, :], p_lo[0:rows, tile % FSLOTS, :], PACK_TILE0 + tile, bank,
                                  False, tile == PACKS - 1, rows, [m])
                last.then_inc(all_summed[m], 1)


def kernel(r_x, L0_rec_W, L0_rec_b, L0_rec_gamma, L0_rec_beta):
    import concourse.bacc as bacc
    import numpy as np
    from concourse.bass_utils import run_bass_kernel_spmd

    nc = bacc.Bacc("TRN2", target_bir_lowering=False, num_devices=1)
    r_x = np.asarray(r_x)
    arrays = {
        "x": np.ascontiguousarray(r_x),
        "x_t": np.ascontiguousarray(r_x.T),
        "sel": selections(),
        "w": np.ascontiguousarray(L0_rec_W),
        "b": np.ascontiguousarray(L0_rec_b).reshape(1, -1),
        "gamma": np.ascontiguousarray(L0_rec_gamma).reshape(1, -1),
        "beta": np.ascontiguousarray(L0_rec_beta).reshape(1, -1),
    }
    args = [nc.dram_tensor(name, a.shape, mybir.dt.from_np(a.dtype), kind="ExternalInput").ap() for name, a in arrays.items()]
    args.append(nc.dram_tensor("out", (BATCH, OUT), F32, kind="ExternalOutput").ap())
    build(nc, *args)
    result = run_bass_kernel_spmd(nc, [arrays], core_ids=[0])
    return result.results[0]["out"]
```
